# Optimizing a Trainium2 kernel written in Bass

```python
import numpy as np
import jax
import jax.numpy as jnp

def _softmax(x, axis=-1):
    return jax.nn.softmax(x, axis=axis)

def _gelu(x):
    return jax.nn.gelu(x, approximate=True)

def _silu(x):
    return jax.nn.silu(x)

def _sigmoid(x):
    return jax.nn.sigmoid(x)

def _layernorm(x, axis=-1, eps=1e-05):
    m = jnp.mean(x, axis=axis, keepdims=True)
    v = jnp.var(x, axis=axis, keepdims=True)
    return (x - m) / jnp.sqrt(v + eps)

def _scatter_add(tgt, idx, src, axis=0):
    return tgt.at[idx].add(src)

def _segment_sum(src, seg, n):
    return jax.ops.segment_sum(src, seg, n)
kernel_name = 'mk_gnn_ffn_d1_gnn_r32_df2a62'

def setup_inputs(seed: int=0):
    np.random.seed(seed)
    _w = jnp.asarray

    def _rec_inputs():
        import jax
        import jax.numpy as jnp
        _gk = jax.random.key(seed)
        x = -8.776e-05 + 1 * jax.random.normal(jax.random.fold_in(_gk, 1), (3125, 256), jnp.float32)
        src = jax.random.randint(jax.random.fold_in(_gk, 2), (50000,), 0, 3125, jnp.int32)
        dst = jnp.minimum((3125 * jax.random.uniform(jax.random.fold_in(_gk, 3), (50000,)) ** 2.0).astype(jnp.int32), 99999)
        _o = jnp.argsort(dst, stable=True)
        src = src[_o]
        dst = dst[_o]
        edge_type_3 = jax.random.randint(jax.random.fold_in(_gk, 12), (50000,), 0, 3, jnp.int32)
        return (x, src, dst, edge_type_3)
    x, src, dst, edge_type_3 = _rec_inputs()

    def _L0_gnn_setup():
        import jax, jax.numpy as jnp
        import numpy as np
        H = 4
        DH = 64
        HID = 256
        EPS = 1e-05
        N_NODES = 625
        N_EDGES = 10000
        N_LAYERS = 3

        def _layer_norm(x, g, b):
            mu = jnp.mean(x, axis=-1, keepdims=True)
            var = jnp.mean((x - mu) ** 2, axis=-1, keepdims=True)
            return (x - mu) * jax.lax.rsqrt(var + EPS) * g + b

        def _message_passing(h, src, tgt, et, Wq, bq, Wk, bk, Wv, bv, Ee, Wo, bo, n_nodes):
            Q = (h @ Wq.T + bq).reshape(-1, H, DH)
            K = (h @ Wk.T + bk).reshape(-1, H, DH)
            V = (h @ Wv.T + bv).reshape(-1, H, DH)
            scores = jnp.einsum('ehd,egd->ehg', Q[src], K[tgt]) / jnp.sqrt(jnp.float32(DH))
            attn = jax.nn.softmax(scores, axis=-1)
            msg = jnp.einsum('ehg,egd->ehd', attn, V[tgt]).reshape(-1, HID)
            msg = msg + Ee[et]
            proj = msg @ Wo.T + bo
            return jax.ops.segment_sum(proj, src, num_segments=n_nodes)
        key = jax.random.key(seed)
        ks = jax.random.split(key, 16)

        def w(k, shape, s=0.05):
            return jax.random.normal(k, shape, jnp.float32) * s
        return {'x': jax.random.normal(ks[0], (N_NODES, HID), jnp.float32), 'edges': jax.random.randint(ks[1], (N_EDGES, 2), 0, N_NODES), 'edge_types': jax.random.randint(ks[2], (N_EDGES,), 0, 3), 'Win': w(ks[3], (HID, HID)), 'b_in': jnp.zeros((HID,), jnp.float32), 'Wq': w(ks[4], (N_LAYERS, HID, HID)), 'bq': jnp.zeros((N_LAYERS, HID), jnp.float32), 'Wk': w(ks[5], (N_LAYERS, HID, HID)), 'bk': jnp.zeros((N_LAYERS, HID), jnp.float32), 'Wv': w(ks[6], (N_LAYERS, HID, HID)), 'bv': jnp.zeros((N_LAYERS, HID), jnp.float32), 'Eemb': w(ks[7], (N_LAYERS, 3, HID)), 'Wo': w(ks[8], (N_LAYERS, HID, HID)), 'bo': jnp.zeros((N_LAYERS, HID), jnp.float32), 'ln_g': jnp.ones((N_LAYERS, HID), jnp.float32), 'ln_b': jnp.zeros((N_LAYERS, HID), jnp.float32), 'W1': w(ks[9], (HID, HID)), 'b1': jnp.zeros((HID,), jnp.float32), 'W2': w(ks[10], (HID, HID)), 'b2': jnp.zeros((HID,), jnp.float32)}
    _L0_gnn_all = _L0_gnn_setup()
    _L0_gnn_in = {k: v for k, v in _L0_gnn_all.items() if k in ('Win', 'b_in', 'Wq', 'bq', 'Wk', 'bk', 'Wv', 'bv', 'Eemb', 'Wo', 'bo', 'ln_g', 'ln_b', 'W1', 'b1', 'W2', 'b2')}
    del _L0_gnn_all

    def _L0_ffn_setup():
        import jax, jax.numpy as jnp
        import numpy as np
        TOP_K = 2
        LN_EPS = 1e-05
        key = jax.random.key(seed)
        ks = jax.random.split(key, 8)
        B, S, D, E, H = (16, 1024, 256, 8, 1024)
        x = jax.random.normal(ks[0], (B, S, D), dtype=jnp.float32)
        Wr = jax.random.normal(ks[1], (D, E), dtype=jnp.float32) * 0.1
        br = jnp.zeros((E,), dtype=jnp.float32)
        ln_g = jnp.ones((E, D), dtype=jnp.float32)
        ln_b = jnp.zeros((E, D), dtype=jnp.float32)
        W1 = jax.random.normal(ks[2], (E, D, H), dtype=jnp.float32) * (1.0 / np.sqrt(D))
        b1 = jnp.zeros((E, H), dtype=jnp.float32)
        W2 = jax.random.normal(ks[3], (E, H, D), dtype=jnp.float32) * (1.0 / np.sqrt(H))
        b2 = jnp.zeros((E, D), dtype=jnp.float32)
        return {'x': x, 'Wr': Wr, 'br': br, 'ln_g': ln_g, 'ln_b': ln_b, 'W1': W1, 'b1': b1, 'W2': W2, 'b2': b2}
    _L0_ffn_all = _L0_ffn_setup()
    _L0_ffn_in = {k: v for k, v in _L0_ffn_all.items() if k in ('Wr', 'br', 'ln_g', 'ln_b', 'W1', 'b1', 'W2', 'b2')}
    del _L0_ffn_all
    return {'x': x, 'src': src, 'dst': dst, 'edge_type_3': edge_type_3, 'L0_gnn_Win': _L0_gnn_in['Win'], 'L0_gnn_b_in': _L0_gnn_in['b_in'], 'L0_gnn_Wq': _L0_gnn_in['Wq'], 'L0_gnn_bq': _L0_gnn_in['bq'], 'L0_gnn_Wk': _L0_gnn_in['Wk'], 'L0_gnn_bk': _L0_gnn_in['bk'], 'L0_gnn_Wv': _L0_gnn_in['Wv'], 'L0_gnn_bv': _L0_gnn_in['bv'], 'L0_gnn_Eemb': _L0_gnn_in['Eemb'], 'L0_gnn_Wo': _L0_gnn_in['Wo'], 'L0_gnn_bo': _L0_gnn_in['bo'], 'L0_gnn_ln_g': _L0_gnn_in['ln_g'], 'L0_gnn_ln_b': _L0_gnn_in['ln_b'], 'L0_gnn_W1': _L0_gnn_in['W1'], 'L0_gnn_b1': _L0_gnn_in['b1'], 'L0_gnn_W2': _L0_gnn_in['W2'], 'L0_gnn_b2': _L0_gnn_in['b2'], 'L0_ffn_Wr': _L0_ffn_in['Wr'], 'L0_ffn_br': _L0_ffn_in['br'], 'L0_ffn_ln_g': _L0_ffn_in['ln_g'], 'L0_ffn_ln_b': _L0_ffn_in['ln_b'], 'L0_ffn_W1': _L0_ffn_in['W1'], 'L0_ffn_b1': _L0_ffn_in['b1'], 'L0_ffn_W2': _L0_ffn_in['W2'], 'L0_ffn_b2': _L0_ffn_in['b2']}

def reference(x, src, dst, edge_type_3, L0_gnn_Win, L0_gnn_b_in, L0_gnn_Wq, L0_gnn_bq, L0_gnn_Wk, L0_gnn_bk, L0_gnn_Wv, L0_gnn_bv, L0_gnn_Eemb, L0_gnn_Wo, L0_gnn_bo, L0_gnn_ln_g, L0_gnn_ln_b, L0_gnn_W1, L0_gnn_b1, L0_gnn_W2, L0_gnn_b2, L0_ffn_Wr, L0_ffn_br, L0_ffn_ln_g, L0_ffn_ln_b, L0_ffn_W1, L0_ffn_b1, L0_ffn_W2, L0_ffn_b2):
    import jax
    import jax.numpy as jnp

    def _L0_gnn_ref(x, edges, edge_types, Win, b_in, Wq, bq, Wk, bk, Wv, bv, Eemb, Wo, bo, ln_g, ln_b, W1, b1, W2, b2):
        import jax, jax.numpy as jnp
        import numpy as np
        H = 4
        DH = 64
        HID = 256
        EPS = 1e-05
        N_NODES = 625
        N_EDGES = 10000
        N_LAYERS = 3

        def _layer_norm(x, g, b):
            mu = jnp.mean(x, axis=-1, keepdims=True)
            var = jnp.mean((x - mu) ** 2, axis=-1, keepdims=True)
            return (x - mu) * jax.lax.rsqrt(var + EPS) * g + b

        def _message_passing(h, src, tgt, et, Wq, bq, Wk, bk, Wv, bv, Ee, Wo, bo, n_nodes):
            Q = (h @ Wq.T + bq).reshape(-1, H, DH)
            K = (h @ Wk.T + bk).reshape(-1, H, DH)
            V = (h @ Wv.T + bv).reshape(-1, H, DH)
            scores = jnp.einsum('ehd,egd->ehg', Q[src], K[tgt]) / jnp.sqrt(jnp.float32(DH))
            attn = jax.nn.softmax(scores, axis=-1)
            msg = jnp.einsum('ehg,egd->ehd', attn, V[tgt]).reshape(-1, HID)
            msg = msg + Ee[et]
            proj = msg @ Wo.T + bo
            return jax.ops.segment_sum(proj, src, num_segments=n_nodes)
        n_nodes = x.shape[0]
        src, tgt = (edges[:, 0], edges[:, 1])
        hidden = x @ Win.T + b_in
        for l in range(N_LAYERS):
            m = _message_passing(hidden, src, tgt, edge_types, Wq[l], bq[l], Wk[l], bk[l], Wv[l], bv[l], Eemb[l], Wo[l], bo[l], n_nodes)
            hidden = jax.nn.relu(_layer_norm(hidden + m, ln_g[l], ln_b[l]))
        adjustment = jax.nn.relu(hidden @ W1.T + b1) @ W2.T + b2
        return x + adjustment

    def _L0_ffn_ref(x, Wr, br, ln_g, ln_b, W1, b1, W2, b2):
        import jax, jax.numpy as jnp
        import numpy as np
        TOP_K = 2
        LN_EPS = 1e-05
        B, S, D = x.shape
        N = B * S
        xt = x.reshape(N, D)
        logits = xt @ Wr + br
        probs = jax.nn.softmax(logits, axis=-1)
        top_p, top_idx = jax.lax.top_k(probs, TOP_K)
        weights = top_p / top_p.sum(axis=-1, keepdims=True)
        mu = xt.mean(axis=-1, keepdims=True)
        var = ((xt - mu) ** 2).mean(axis=-1, keepdims=True)
        xn = (xt - mu) * jax.lax.rsqrt(var + LN_EPS)
        xe = xn[None, :, :] * ln_g[:, None, :] + ln_b[:, None, :]
        h = jax.nn.gelu(jnp.einsum('end,edh->enh', xe, W1) + b1[:, None, :], approximate=False)
        y = jnp.einsum('enh,ehd->end', h, W2) + b2[:, None, :]
        y_tok = jnp.transpose(y, (1, 0, 2))
        sel = jnp.take_along_axis(y_tok, top_idx[:, :, None], axis=1)
        out = (weights[:, :, None] * sel).sum(axis=1)
        return out.reshape(B, S, D)
    edge_index_t = jnp.stack([src, dst], axis=1)
    x = x + _L0_gnn_ref(_layernorm(x, axis=-1), edge_index_t, edge_type_3, L0_gnn_Win, L0_gnn_b_in, L0_gnn_Wq, L0_gnn_bq, L0_gnn_Wk, L0_gnn_bk, L0_gnn_Wv, L0_gnn_bv, L0_gnn_Eemb, L0_gnn_Wo, L0_gnn_bo, L0_gnn_ln_g, L0_gnn_ln_b, L0_gnn_W1, L0_gnn_b1, L0_gnn_W2, L0_gnn_b2)
    x = x + _L0_ffn_ref(_layernorm(x, axis=-1)[None], L0_ffn_Wr, L0_ffn_br, L0_ffn_ln_g, L0_ffn_ln_b, L0_ffn_W1, L0_ffn_b1, L0_ffn_W2, L0_ffn_b2)[0]
    return x

_drawn_inputs = setup_inputs


def setup_inputs(seed=0):
    import zlib

    import numpy as np

    out = dict(_drawn_inputs(seed))
    spreads = {'L0_gnn_b_in': (0.0, 0.1),
     'L0_gnn_bq': (0.0, 0.47),
     'L0_gnn_bk': (0.0, 0.465),
     'L0_gnn_bv': (0.0, 0.1),
     'L0_gnn_bo': (0.0, 0.1),
     'L0_gnn_ln_g': (1.0, 0.2),
     'L0_gnn_ln_b': (0.0, 0.1),
     'L0_gnn_b1': (0.0, 0.1),
     'L0_gnn_b2': (0.0, 0.1),
     'L0_ffn_br': (0.0, 0.1),
     'L0_ffn_ln_g': (1.0, 0.2),
     'L0_ffn_ln_b': (0.0, 0.31),
     'L0_ffn_b1': (0.0, 0.306),
     'L0_ffn_b2': (0.0, 0.1)}
    factors = {}
    for name, (base, spread) in spreads.items():
        noise = np.random.default_rng([zlib.crc32(name.encode()), seed]).standard_normal(out[name].shape)
        drawn = base * np.exp(spread * noise) if base else spread * noise
        out[name] = jnp.asarray(drawn.astype(out[name].dtype))
    for name, factor in factors.items():
        out[name] = (out[name] * factor).astype(out[name].dtype)
    return out
```

```python
from collections import namedtuple
from contextlib import ExitStack

import numpy as np
import concourse.bass as bass
from concourse import mybir

ALU = mybir.AluOpType
ACT = mybir.ActivationFunctionType
AX = mybir.AxisListType
F32 = mybir.dt.float32
BF16 = mybir.dt.bfloat16
I32 = mybir.dt.int32
ds = bass.ds

P = 128
N, D, H, DH, E, L = 3125, 256, 4, 64, 50000, 3
NT = -(-N // P)
NP = NT * P
G = 5
NG = NT // G
W = 16
NW = NP // W
EC = -(-E // P)
EF = E // P
ER = E - EF * P
CH = 13
NCH = EF // CH
UB = 4
TURN = 4
ET = -(-(E // P + -(-N // W)) // (UB * TURN)) * UB * TURN
NB = ET // UB
NTURN = NB // TURN
TG = 8
KC = D // P
BIG = float(2.0 ** 100)
EPS = 1e-5
X = 8
HID = 1024
HC = HID // P
MT = -(-(2 * N + X * (P - 1)) // P)
TYPES = 4
MT += MT % 2
PACK = KC * HID + 2 * KC + HC + D
assert NT % G == 0 and EF % (2 * CH) == 0 and ET >= (E + -(-N // W) * (P - 1)) // P


KN = 2 * G + 1
NOB = -(-(ET // TG) // 8)
SC0 = NCH // 2 * CH * 16
ROWS_F = NG * (1 + 2 * L) * 16
ROWS_C = ROWS_F + NG * 32
NWL = 9


def build(nc, A, out):
    ctx = ExitStack()
    with ctx:
        def sb(name, shape, dt=F32):
            return ctx.enter_context(nc.sbuf_tensor(name, shape, dt))

        def sem(name):
            return ctx.enter_context(nc.semaphore(name))

        def dram(name, shape, dt=F32):
            return nc.dram_tensor(name, shape, dt, kind="Internal").ap()

        hid_d = dram("hid_d", [NP, D])
        kv_d = dram("kv_d", [NP, 2 * D])
        rec_d = dram("rec_d", [P * ET, 2], I32)
        wid_d = dram("wid_d", [P * 5], I32)

        ident = sb("ident", [P, P])
        identb = sb("identb", [P, P], BF16)
        below = sb("below", [P, P], BF16)
        notbelow = sb("notbelow", [P, P], BF16)
        iotab = sb("iotab", [P, NW], BF16)
        tileid = sb("tileid", [P, 5])
        maskc = sb("maskc", [P, TG, D], BF16)
        epsc = sb("epsc", [P, 1])
        onesrow = sb("onesrow", [1, P])
        zerob = sb("zerob", [P, P], BF16)

        n_kv, n_qa, n_oh = TURN * UB * 2 * D, NW * W * H, ET * W // 2
        o_qa, o_oh = n_kv, n_kv + n_qa
        o_cnt = o_oh + 2 * n_oh
        arena = sb("arena", [P, o_cnt + NT * P])
        qa = arena[:, o_qa:o_oh].rearrange("p (w x) -> p w x", w=NW)
        qt, acc = qa[0:DH], qa[DH:P]
        kv = arena[:, 0:n_kv].rearrange("p (b u n) -> p b u n", b=TURN, u=UB)
        gidx = sb("gidx", [P, TURN, UB], I32)
        kt_s = sb("kt_s", [P, 2, KC, P])
        qbd = sb("qbd", [P, 2, P])
        sc = sb("sc", [P, 2, UB, H, H])
        mx = sb("mx", [P, 2, UB, H])
        sx = sb("sx", [P, 2, UB, H, H])
        ex = sb("ex", [P, 2, UB, H, H])
        sm = sb("sm", [P, 2, UB, H])
        rc = sb("rc", [P, 2, UB, H])
        at = sb("at", [P, 2, UB, H, H])
        att = sb("att", [P, 2, UB, W, H, H])

        selq = arena[:, o_cnt:o_cnt + P // W * P].rearrange("p (q n) -> p q n", q=P // W)
        early = arena[:, 0:n_kv]
        early_b = early.bitcast(BF16)
        n_lo, n_code, n_win = 2 * CH * P, 2 * CH * NT * TYPES, 2 * CH * NW
        oh_lo = early_b[:, 0:n_lo].rearrange("p (b k n) -> p b k n", b=2, k=CH)
        oh_code = early_b[:, n_lo:n_lo + n_code].rearrange("p (b k n) -> p b k n", b=2, k=CH)
        oh_win = early_b[:, n_lo + n_code:n_lo + n_code + n_win].rearrange("p (b k n) -> p b k n", b=2, k=CH)
        at_f = (n_lo + n_code + n_win) // 2
        lo_f, code_f, win_f = (early[:, at_f + k * EC:at_f + (k + 1) * EC] for k in range(3))
        idx_in = early[:, at_f + 3 * EC:at_f + 6 * EC].bitcast(I32).rearrange("p (a c) -> p a c", a=3)
        sorting = arena[:, o_oh:o_oh + 4 * EC].bitcast(I32)
        tmp_i, slot_all = sorting[:, 0:EC], sorting[:, EC:2 * EC]
        pay = sorting[:, 2 * EC:].rearrange("p (c x) -> p c x", x=2)
        cnt_a = sb("cnt_a", [P, NT, TYPES])
        cnt4 = sb("cnt4", [P, NT, TYPES])
        cnt_hi = sb("cnt_hi", [P, 2, NT])
        wt_i = sb("wt_i", [P, 2, NW], I32)
        wt_f = sb("wt_f", [P, NW])
        wt_end = sb("wt_end", [P, NW])
        wt_start = sb("wt_start", [P, NW])
        wt_one = sb("wt_one", [P, NW])
        wt_base = sb("wt_base", [P, 2, NW])
        wid_f = sb("wid_f", [P, 5])
        wid_i = sb("wid_i", [P, 5], I32)
        wid = sb("wid", [1, ET], I32)
        code_s = sb("code_s", [P, 2, CH])
        rank = sb("rank", [P, 2, CH])
        rank_i = sb("rank_i", [P, 3, CH], I32)
        slot_s = sb("slot_s", [P, 2, CH], I32)
        pay_s = sb("pay_s", [P, 2, CH, 2], I32)
        junk = sb("junk", [P, 2, NW])
        cntT = arena[0:TYPES, o_cnt:o_cnt + NT * P].rearrange("p (t n) -> p t n", n=P)
        rec = sb("rec", [P, ET, 2], I32)
        onehot = arena[:, o_oh:o_oh + n_oh].bitcast(BF16).rearrange("p (t s) -> p t s", s=W)
        ohT = arena[:, o_oh + n_oh:o_cnt].bitcast(BF16).rearrange("p (t n) -> p t n", n=P)

        xin = sb("xin", [P, G, D])
        xT = sb("xT", [P, G, KC, P])
        x0 = early[:, G * 2 * D:G * 3 * D].rearrange("p (j n) -> p j n", j=G)
        st = sb("st", [P, G, 6])
        mv = sb("mv", [P, G, 2])
        sd = sb("sd", [P, G])
        rs = sb("rs", [P, G])
        hout = early[:, G * 3 * D:G * 4 * D].rearrange("p (j n) -> p j n", j=G)
        kvout = early[:, 0:G * 2 * D].rearrange("p (j n) -> p j n", j=G)
        w_in = sb("w_in", [P, KC, D])
        b_in = sb("b_in", [P, D])
        wq = sb("wq", [P, KC, D])
        bq = sb("bq", [P, KC])
        bq8 = sb("bq8", [P, KC])
        wkv = sb("wkv", [P, KC, 2 * D])
        bkv = sb("bkv", [P, 2 * D])
        wo = sb("wo", [P, KC, D])
        eeT = sb("eeT", [P, KC, TYPES])
        bo4 = sb("bo4", [TYPES, D])
        eewo = sb("eewo", [TYPES, D])
        lng = sb("lng", [P, D])
        lnb = sb("lnb", [P, D])
        aggT = xT
        cnt_s = early[0:TYPES, G * 4 * D:G * 4 * D + G * P].rearrange("p (j n) -> p j n", j=G)

        o_w2 = 6144
        o_f = o_w2 + X * HC * D
        w2r = arena[:, o_w2:o_f].rearrange("p (e c n) -> p e c n", e=X, c=HC)
        xo = arena[:, o_f:o_f + G * D].rearrange("p (j n) -> p j n", j=G)
        rT = arena[:, o_f + G * D:o_f + 2 * G * D].rearrange("p (j c n) -> p j c n", j=G, c=KC)
        o_w1 = o_f + 2 * G * D
        w1s = arena[:, o_w1:o_w1 + 2 * PACK].rearrange("p (b n) -> p b n", b=2)
        zb = early[:, 0:G * D].rearrange("p (j n) -> p j n", j=G)
        xnb = early[:, G * D:2 * G * D].rearrange("p (j n) -> p j n", j=G)
        hs = early[:, 0:2 * HID].rearrange("p (b c n) -> p b c n", b=2, c=HC)
        assert o_w1 + 2 * PACK <= o_cnt

        def small(k):
            return arena[:, o_cnt + k * NT * X:o_cnt + (k + 1) * NT * X].rearrange("p (t e) -> p t e", e=X)

        wf1, wf2 = (early[:, 5120 + k * KC * D:5120 + (k + 1) * KC * D].rearrange("p (c n) -> p c n", c=KC) for k in range(2))
        o_s = o_w1 + 2 * PACK
        bf2 = arena[:, o_s:o_s + D]
        scan0 = arena[:, o_s + D:o_s + D + NT * X]
        lg = arena[:, o_s + D + NT * X:o_s + D + 2 * NT * X].rearrange("p (t e) -> p t e", e=X)
        bf1 = sb("bf1", [P, KC])
        wr = sb("wr", [P, KC, X])
        brw = sb("brw", [P, X])
        valid = sb("valid", [P, NT])
        tokid = sb("tokid", [P, NT], I32)
        tileid0 = sb("tileid0", [P, 1])
        iotax = sb("iotax", [P, X])
        onesb = sb("onesb", [P, P], BF16)
        cols = sb("cols", [P, 8, NT])
        slot_f = sb("slot_f", [P, 2, NT])
        slot2 = sb("slot2", [P, 2, NT], I32)
        tok_at = sb("tok_at", [P, 3, 2, NT], I32)
        oex = sb("oex", [P, 2, X, NT], BF16)
        et = sb("et", [P, 6, X])
        et_i = sb("et_i", [P, 2, X], I32)
        eid_f = sb("eid_f", [P, 1])
        eid_i = sb("eid_i", [P, 1], I32)
        eid = sb("eid", [1, 64], I32)
        tokl = sb("tokl", [P, MT], I32)
        tok_s = sb("tok_s", [P, 2], I32)
        wcol = sb("wcol", [P, G, 2])
        yidx = sb("yidx", [P, G, 2], I32)
        x1_d = dram("x1_d", [NP, D])
        xn_d = dram("xn_d", [NP, D])
        tok_d = dram("tok_d", [P * MT, 1], I32)
        eid_d = dram("eid_d", [P], I32)
        y_d = dram("y_d", [P * MT, D])

        bank = [ctx.enter_context(nc.psum_tensor(f"bank{i}", [P, 512], F32)) for i in range(8)]
        bank_b = [b[:, :].bitcast(BF16) for b in bank]

        names = ("const_landed idx_landed start_ready spare fields_ready ohlo_ready ohcode_ready hist_used "
                 "hist_done hist_copied wincnt_done base_ready ohwin_ready rank_ready rank_read "
                 "slot_ready rec_blank rec_filled wid_ready wid_stored wid_landed rec_landed onehot_ready "
                 "ranks_all code_copied oht_done oht_copied cnt_done cnt_copied chain_s chain_r slot_copied "
                 " chain_in mean_ready std_ready x0_ready xT_done xT_ready proj_done hout_ready "
                 "wl_landed bias_ready  hT_done hT_ready q_done q_ready kvp_done kvp_ready "
                 "ee_done ee_ready sums_zeroed sums_copied  "
                 "idx_ready kT_done kT_ready score_done score_read exp_in exp_out att_ready chain_e chain_a "
                 "agg_done edges_all  cnts_ready upd_done chain_u mean_u std_u x0_u h_u  "
                 "f_hT_done f_xT_ready f_u_done f_r_ready f_adj_done chain_f f_std f_x0 f_xs chain_y f_x1 f_z f_xn f_zT_done "
                 "f_zT_ready f_lg_done f_lg_ready r_exp r_exped chain_x r_occ r_rank r_slots w2_landed tok_blank "
                 "tok_filled tok_scattered eid_stored eid_landed tokl_landed "
                 "m_idx m_xT_done m_xe_ready m_h_done m_h_ready m_y_done m_y_ready "
                 "c_idx c_part c_out").split()
        S = namedtuple("Semaphores", names)(*[sem(n) for n in names])
        rows_landed = [sem(f"rows_landed{j}") for j in range(G)]
        rows_stored = [sem(f"rows_stored{j}") for j in range(G)]
        gathered = [sem(f"gathered{k}") for k in range(TURN * UB)]
        h_stored = [sem(f"h_stored{j}") for j in range(G)]
        kvo_stored = [sem(f"kvo_stored{j}") for j in range(G)]
        scattered = [sem(f"scattered{b}") for b in range(2)]
        m_w1_landed = [sem(f"m_w1_landed{p}") for p in range(2)]
        y_stored = [sem(f"y_stored{p}") for p in range(2)]

        consts = [(w_in[:, :, :], A.win), (b_in[:, :], A.b_in), (ident[:, :], A.c_ident), (identb[:, :], A.c_identb),
                  (below[:, :], A.c_below), (notbelow[:, :], A.c_notbelow), (selq, A.c_selq),
                  (iotab[:, :], A.c_iota), (tileid[:, :], A.c_tileid), (maskc[:, :, :], A.c_mask),
                  (onesrow[:, :], A.c_ones), (zerob[:, :], A.c_zero), 
                  (bf1[:, :], A.bf1), (wr[:, :, :], A.wr), (brw[:, :], A.br),
                  (valid[:, :], A.c_valid), (tokid[:, :], A.c_tokid), (iotax[:, :], A.c_iotax),
                  (onesb[:, :], A.c_onesb), (tileid0[:, :], A.c_tile0)]
        late = [(wf1, A.wf1), (wf2, A.wf2), (bf2, A.bf2), (scan0, A.c_scan0), (w2r, A.w2)]
        layer_weights = [(wq[:, :, :], A.wq), (bq[:, :], A.bq), (wkv[:, :, :], A.wkv), (bkv[:, :], A.bkv),
                         (wo[:, :, :], A.wo), (eeT[:, :, :], A.eeT), (bo4[:, :], A.bo4), (lng[:, :], A.lng), (lnb[:, :], A.lnb)]

        def hold(eng, s, value):
            eng.wait_ge(s, value)
            eng.sem_inc(S.spare, 1)

        nconst = len(consts)

        def rows(t):
            return ds(t * P, P)

        block = ctx.enter_context(nc.Block())

        @block.sync
        def _(sp):
            sp.dma_start(idx_in, A.edges).then_inc(S.idx_landed, 16)
            for dst, src in consts:
                sp.dma_start(dst, src).then_inc(S.const_landed, 16)
            sp.wait_ge(S.rec_blank, 2)
            sp.dma_start(rec_d.rearrange("(p t) x -> p t x", p=P), rec[:, :, :]).then_inc(S.rec_filled, 16)

            def load_x(i):
                for j in range(G):
                    n = i * G + j
                    hold(sp, S.x0_ready, n + 1)
                    sp.dma_start(xin[:, j, :], A.x[rows(n), :]).then_inc(rows_landed[j], 16)

            def store_h(i, base):
                for j in range(G):
                    n = i * G + j
                    hold(sp, S.hout_ready, base + n + 1)
                    sp.dma_start(hid_d[rows(n), :], hout[:, j, :]).then_inc(h_stored[j], 16)

            sp.wait_ge(S.start_ready, 1)
            load_x(0)
            sp.wait_ge(S.wid_ready, 1)
            sp.dma_start(wid_d.rearrange("(p k) -> p k", p=P), wid_i[:, :]).then_inc(S.wid_stored, 16)
            sp.wait_ge(S.wid_stored, 16)
            sp.dma_start(wid[:, :], wid_d[0:ET].rearrange("(a t) -> a t", a=1)).then_inc(S.wid_landed, 16)
            with nc.sync.Fori(1, NG) as i:
                load_x(i)
                store_h(i - 1, 0)
            store_h(NG - 1, 0)

            def q_loads(l, i):
                for j in range(G):
                    n = i * G + j
                    hold(sp, S.hT_done, l * NT + n + 1)
                    sp.dma_start(xin[:, j, :], hid_d[rows(n), :]).then_inc(rows_landed[j], 16)

            def q_stores(l, i):
                for j in range(G):
                    n = i * G + j
                    hold(sp, S.kvp_ready, l * NT + n + 3)
                    sp.dma_start(kv_d[rows(n), :], kvout[:, j, :]).then_inc(kvo_stored[j], 16)

            def q_phase(l):
                for j in range(G):
                    hold(sp, h_stored[j], (l + 1) * NG * 16 + 16)
                for dst, src in layer_weights:
                    sp.dma_start(dst, src[ds(l, 1)].squeeze(0) if not isinstance(l, int) else src[l]).then_inc(S.wl_landed, 16)
                q_loads(l, 0)
                with nc.sync.Fori(1, NG) as i:
                    q_loads(l, i)
                    q_stores(l, i - 1)
                q_stores(l, NG - 1)

            def u_phase(l):
                hold(sp, S.edges_all, l + 1)
                for j in range(G):
                    sp.dma_start(xin[:, j, :], hid_d[j * P:(j + 1) * P, :]).then_inc(rows_landed[j], 16)
                with nc.sync.Fori(1, NG) as i:
                    store_h(i - 1, (l + 1) * NT)
                    for j in range(G):
                        n = i * G + j
                        sp.dma_start(xin[:, j, :], hid_d[rows(n), :]).then_inc(rows_landed[j], 16)
                store_h(NG - 1, (l + 1) * NT)

            q_phase(0)
            sp.wait_ge(scattered[0], SC0 + 16)
            sp.wait_ge(scattered[1], SC0)
            sp.dma_start(rec[:, :, :], rec_d.rearrange("(p t) x -> p t x", p=P)).then_inc(S.rec_landed, 16)
            with nc.sync.Fori(0, L - 1) as l:
                u_phase(l)
                q_phase(l + 1)
            u_phase(L - 1)
            for j in range(G):
                sp.wait_ge(h_stored[j], (L + 1) * NG * 16 + 16)
            sp.wait_ge(S.sums_copied, (L + 1) * NT)
            for dst, src in late:
                sp.dma_start(dst, src).then_inc(S.w2_landed, 16)

            def f_loads(i):
                for j in range(G):
                    n = i * G + j
                    hold(sp, S.f_hT_done, n + 1)
                    hold(sp, S.f_xs, i + 1)
                    sp.dma_start(xin[:, j, :], hid_d[rows(n), :]).then_inc(rows_landed[j], 16)
                    sp.dma_start(xo[:, j, :], A.x[rows(n), :]).then_inc(rows_landed[j], 16)

            def f_stores(i):
                for j in range(G):
                    n = i * G + j
                    hold(sp, S.f_xn, n + 1)
                    sp.dma_start(x1_d[rows(n), :], hout[:, j, :]).then_inc(rows_stored[j], 16)
                    sp.dma_start(xn_d[rows(n), :], xnb[:, j, :]).then_inc(rows_stored[j], 16)

            f_loads(0)
            with nc.sync.Fori(1, NG) as i:
                f_loads(i)
                f_stores(i - 1)
            f_stores(NG - 1)
            sp.wait_ge(S.tok_blank, 1)
            sp.dma_start(tok_d.rearrange("(p t) x -> p (t x)", p=P), tokl[:, :]).then_inc(S.tok_filled, 16)
            sp.wait_ge(S.r_slots, 1)
            sp.dma_start(eid_d.rearrange("(p a) -> p a", a=1), eid_i[:, :]).then_inc(S.eid_stored, 16)
            sp.wait_ge(S.eid_stored, 16)
            sp.dma_start(eid[:, :], eid_d[0:64].rearrange("(a t) -> a t", a=1)).then_inc(S.eid_landed, 16)
            sp.wait_ge(S.tok_scattered, 2 * NT * 16)
            sp.dma_start(tokl[:, :], tok_d.rearrange("(p t) x -> p (t x)", p=P)).then_inc(S.tokl_landed, 16)
            sp.wait_ge(S.eid_landed, 16)
            sreg = [sp.alloc_register(f"ws{p}") for p in range(2)]

            def w1_load(m, p, r):
                sp.dma_start(w1s[:, p, :], A.pack[ds(sp.snap(sreg[r]), 1)].squeeze(0)).then_inc(m_w1_landed[p], 16)

            sp.load(sreg, eid[0:1, 0:2])
            for p in range(2):
                w1_load(p, p, p)

            def m_turn(i, last):
                if not last:
                    sp.load(sreg, eid[0:1, ds(i * 2 + 2, 2)])
                for p in range(2):
                    m = 2 * i + p
                    hold(sp, S.m_y_ready, m + 1)
                    if not last:
                        w1_load(m + 2, p, p)
                    sp.dma_start(y_d[ds(m * P, P), :], hout[:, p, :]).then_inc(y_stored[p], 16)

            with nc.sync.Fori(0, MT // 2 - 1) as i:
                m_turn(i, False)
            m_turn(MT // 2 - 1, True)

            def c_loads(i):
                for j in range(G):
                    n = i * G + j
                    hold(sp, S.c_part, n + 1)
                    sp.dma_start(xo[:, j, :], x1_d[rows(n), :]).then_inc(rows_landed[j], 16)

            def c_stores(i):
                for j in range(G):
                    n = i * G + j
                    hold(sp, S.c_out, n + 1 + G)
                    sp.dma_start(out[rows(n), :], xin[:, j, :]).then_inc(rows_stored[j], 16)

            c_loads(0)
            with nc.sync.Fori(1, NG) as i:
                c_loads(i)
                c_stores(i - 1)
            c_stores(NG - 1)
            for j in range(G):
                sp.wait_ge(rows_stored[j], NG * 48 + 32)

        @block.gpsimd
        def _(pool):
            pool.memset(rec[:, :, 0:1], 0).then_inc(S.rec_blank, 1)
            pool.memset(rec[:, :, 1:2], W).then_inc(S.rec_blank, 1)
            for s, k in ((S.hist_used, 2), (S.x0_ready, G), (S.hT_done, G), (S.q_ready, G), (S.kvp_ready, 2),
                         (S.sums_copied, NT), (S.agg_done, TURN), (S.upd_done, G), (S.h_u, G), (S.score_read, 4)):
                pool.sem_inc(s, k)
            for s, k in ((S.f_hT_done, G), (S.f_xs, 1), (S.c_part, G), (S.m_y_done, 2)):
                pool.sem_inc(s, k)
            for j in range(G):
                pool.sem_inc(rows_stored[j], 32)
            for p in range(2):
                pool.sem_inc(y_stored[p], 16)
            for j in range(G):
                pool.sem_inc(h_stored[j], 16)
                pool.sem_inc(kvo_stored[j], 16)
            pool.sem_inc(S.start_ready, 1)
            pool.wait_ge(S.const_landed, 16 * nconst)
            pool.wait_ge(S.fields_ready, 1)

            def one_hot_code(c, b, k0, n):
                hold(pool, S.hist_used, c + 1)
                pool.tensor_copy(code_s[:, b, 0:n], code_f[:, ds(k0, n)]).then_inc(S.code_copied, 1)
                hold(pool, S.code_copied, c + 1)
                for k in range(n):
                    ins = pool.tensor_scalar(oh_code[:, b, k, :], iotab[:, 0:NT * TYPES], code_s[:, b, k:k + 1], None,
                                             ALU.is_equal)
                ins.then_inc(S.ohcode_ready, 1)

            with nc.gpsimd.Fori(0, NCH // 2) as i:
                for b in range(2):
                    one_hot_code(2 * i + b, b, (2 * i + b) * CH, CH)
            one_hot_code(NCH, 0, EF, 1)

            pool.wait_ge(S.rec_filled, 16)

            def scatter(c, b, k0, n, r):
                hold(pool, S.slot_ready, c + 1)
                pool.tensor_copy(slot_s[:, b, 0:n], slot_all[:, ds(k0, n)]).then_inc(S.slot_copied, 1)
                pool.tensor_copy(pay_s[:, b, 0:n, :], pay[:, ds(k0, n), :]).then_inc(S.slot_copied, 1)
                hold(pool, S.slot_copied, 2 * c + 2)
                for k in range(n):
                    pool.indirect_dma_start(
                        rec_d, bass.IndirectOffsetOnAxis(slot_s[0:r, b, k:k + 1], 0), pay_s[0:r, b, k, :], None,
                    ).then_inc(scattered[b], 16)

            scatter(0, 0, 0, CH, P)
            scatter(1, 1, CH, CH, P)
            with nc.gpsimd.Fori(1, NCH // 2) as i:
                for b in range(2):
                    hold(pool, scattered[b], i * CH * 16)
                    scatter(2 * i + b, b, (2 * i + b) * CH, CH, P)
            pool.wait_ge(scattered[0], SC0)
            scatter(NCH, 0, EF, 1, ER)
            pool.wait_ge(S.rec_landed, 16)

            def e_phase(l):
                hold(pool, S.sums_copied, (l + 1) * NT)
                pool.memset(acc, 0.0).then_inc(S.sums_zeroed, 1)
                hold(pool, S.sums_zeroed, l + 1)
                for j in range(G):
                    hold(pool, kvo_stored[j], (l + 1) * NG * 16 + 16)
                with nc.gpsimd.Fori(0, NTURN) as i:
                    for b in range(TURN):
                        n = l * NB + i * TURN + b
                        hold(pool, S.agg_done, n + 1)
                        pool.tensor_copy(gidx[:, b, :], rec[:, ds((i * TURN + b) * UB, UB), 0]).then_inc(S.idx_ready, 1)
                        hold(pool, S.idx_ready, n + 1)
                        for u in range(UB):
                            pool.indirect_dma_start(
                                kv[:, b, u, :], None, kv_d, bass.IndirectOffsetOnAxis(gidx[:, b, u:u + 1], 0),
                            ).then_inc(gathered[b * UB + u], 16)

            def u_phase(l):
                hold(pool, S.edges_all, l + 1)
                with nc.gpsimd.Fori(0, NG) as i:
                    for j in range(G):
                        n = i * G + j
                        hold(pool, S.upd_done, l * NT + n + 1)
                        pool.tensor_copy(cnt_s[:, j, :], cntT[:, ds(n, 1), :].squeeze(1)).then_inc(S.cnts_ready, 1)

            with nc.gpsimd.Fori(0, L - 1) as l:
                e_phase(l)
                u_phase(l)
            e_phase(L - 1)
            u_phase(L - 1)

            pool.memset(tokl[:, :], 0).then_inc(S.tok_blank, 1)
            pool.wait_ge(S.tok_filled, 16)
            pool.wait_ge(S.r_slots, 1)
            for t in range(NT):
                r = min(P, N - t * P)
                for k in range(2):
                    pool.indirect_dma_start(
                        tok_d, bass.IndirectOffsetOnAxis(tok_at[0:r, 2, k, t:t + 1], 0), tokid[0:r, t:t + 1], None,
                    ).then_inc(S.tok_scattered, 16)
            pool.wait_ge(S.tokl_landed, 16)

            def m_gather(m, p):
                pool.tensor_copy(tok_s[:, p:p + 1], tokl[:, ds(m, 1)]).then_inc(S.m_idx, 1)
                hold(pool, S.m_idx, m + 1)
                pool.indirect_dma_start(xin[:, p, :], None, xn_d, bass.IndirectOffsetOnAxis(tok_s[:, p:p + 1], 0),
                                        ).then_inc(gathered[G + p], 16)

            for p in range(2):
                m_gather(p, p)
            with nc.gpsimd.Fori(1, MT // 2) as i:
                for p in range(2):
                    hold(pool, S.m_xT_done, 2 * i + p - 1)
                    m_gather(2 * i + p, p)
            for p in range(2):
                pool.wait_ge(y_stored[p], MT // 2 * 16 + 16)
            with nc.gpsimd.Fori(0, NG) as i:
                hold(pool, S.c_out, i * G + G)
                pool.tensor_copy(yidx[:, :, :], slot2[:, :, ds(i * G, G)].rearrange("p k t -> p t k")).then_inc(S.c_idx, 1)
                pool.tensor_copy(wcol[:, :, :], cols[:, 6:8, ds(i * G, G)].rearrange("p k t -> p t k")).then_inc(S.c_idx, 1)
                hold(pool, S.c_idx, 2 * i + 2)
                for j in range(G):
                    for k in range(2):
                        pool.indirect_dma_start(
                            (zb if k == 0 else xnb)[:, j, :], None, y_d, bass.IndirectOffsetOnAxis(yidx[:, j, k:k + 1], 0),
                        ).then_inc(gathered[j], 16)

        @block.vector
        def _(dve):
            dve.memset(epsc[:, :], EPS).then_inc(S.chain_s, 1)
            dve.memset(wt_one[:, :], 1.0).then_inc(S.chain_s, 1)
            dve.memset(qbd[:, :, :], 0.0).then_inc(S.chain_s, 1)
            cs = [3]

            def link(ins):
                cs[0] += 1
                ins.then_inc(S.chain_s, 1)
                dve.wait_ge(S.chain_s, cs[0])

            dve.wait_ge(S.idx_landed, 16)
            src, dst, typ = idx_in[:, 0, :], idx_in[:, 1, :], idx_in[:, 2, :]
            link(dve.tensor_scalar(tmp_i, src, 7, None, ALU.arith_shift_right))
            link(dve.scalar_tensor_tensor(out=code_f, in0=tmp_i, scalar=float(TYPES), in1=typ,
                                          op0=ALU.mult, op1=ALU.add))
            link(dve.tensor_scalar(tmp_i, src, P - 1, None, ALU.bitwise_and))
            link(dve.tensor_copy(lo_f, tmp_i))
            link(dve.tensor_scalar(tmp_i, src, 4, None, ALU.arith_shift_right))
            link(dve.tensor_copy(win_f, tmp_i))
            link(dve.tensor_scalar(tmp_i, src, W - 1, None, ALU.bitwise_and))
            link(dve.tensor_copy(pay[:, :, 1], tmp_i))
            dve.tensor_copy(pay[:, :, 0], dst).then_inc(S.fields_ready, 1)
            dve.wait_ge(S.const_landed, 16 * nconst)
            dve.wait_ge(S.start_ready, 1)

            def one_hot_lo(c, b, k0, n):
                hold(dve, S.hist_used, c + 1)
                dve.tensor_tensor(
                    oh_lo[:, b, 0:n, :], iotab[:, 0:P].unsqueeze(1).to_broadcast([P, n, P]),
                    lo_f[:, ds(k0, n)].unsqueeze(2).to_broadcast([P, n, P]), ALU.is_equal,
                ).then_inc(S.ohlo_ready, 1)

            with nc.vector.Fori(0, NCH // 2) as i:
                for b in range(2):
                    one_hot_lo(2 * i + b, b, (2 * i + b) * CH, CH)
            one_hot_lo(NCH, 0, EF, 1)

            dve.wait_ge(S.hist_done, 1)
            link(dve.tensor_copy(cnt_a[:, :, :], bank[0][:, 0:NT * TYPES].rearrange("p (t y) -> p t y", y=TYPES)))
            link(dve.tensor_tensor(cnt4[:, :, :], cnt_a[:, :, :],
                                   bank[1][:, 0:NT * TYPES].rearrange("p (t y) -> p t y", y=TYPES), ALU.add))
            link(dve.reduce_sum(cnt_hi[:, 0, :], cnt4[:, :, :], AX.X))
            link(dve.reduce_sum(cnt_hi[:, 1, :], cnt_a[:, :, :], AX.X))
            link(dve.tensor_copy(cnt4[:, :, TYPES - 1], cnt_hi[:, 0, :]))
            dve.sem_inc(S.hist_copied, 1)
            dve.wait_ge(S.wincnt_done, 1)
            link(dve.tensor_scalar(wt_i[:, 0, :], bank[2][:, 0:NW], float(P - 1), None, ALU.add))
            link(dve.tensor_scalar(wt_i[:, 1, :], wt_i[:, 0, :], 7, None, ALU.arith_shift_right))
            link(dve.tensor_copy(wt_f[:, :], wt_i[:, 1, :]))
            link(dve.tensor_tensor_scan(wt_end[:, :], wt_one[:, :], wt_f[:, :], 0.0, ALU.mult, ALU.add))
            link(dve.tensor_tensor(wt_start[:, :], wt_end[:, :], wt_f[:, :], ALU.subtract))
            link(dve.tensor_scalar(wt_base[:, 0, :], wt_start[:, :], float(P), None, ALU.mult))
            dve.tensor_tensor(wt_base[:, 1, :], wt_base[:, 0, :], bank[3][:, 0:NW], ALU.add).then_inc(S.base_ready, 1)
            for k in range(5):
                link(dve.tensor_scalar(junk[:, 0, :], wt_start[:, :], tileid[:, k:k + 1], None, ALU.is_le, ALU.add,
                                       accum_out=wid_f[:, k:k + 1]))
            dve.tensor_scalar(wid_i[:, :], wid_f[:, :], -1.0, None, ALU.add).then_inc(S.wid_ready, 1)

            def slots(c, b, k0, n):
                dve.tensor_tensor(
                    oh_win[:, b, 0:n, :], iotab[:, :].unsqueeze(1).to_broadcast([P, n, NW]),
                    win_f[:, ds(k0, n)].unsqueeze(2).to_broadcast([P, n, NW]), ALU.is_equal,
                ).then_inc(S.ohwin_ready, 1)
                dve.wait_ge(S.ohwin_ready, c + 1)
                for k in range(n):
                    e = c * CH + k
                    dve.wait_ge(S.rank_ready, e + 1)
                    dve.tensor_tensor_reduce(out=junk[:, k % 2, :], in0=bank[4 + k % 2][:, 0:NW], in1=oh_win[:, b, k, :],
                                             scale=1.0, scalar=0.0, op0=ALU.mult, op1=ALU.add,
                                             accum_out=rank[:, b, k:k + 1]).then_inc(S.rank_read, 1)
                dve.wait_ge(S.rank_read, c * CH + n)
                r = 3 * c
                dve.tensor_copy(rank_i[:, 0, 0:n], rank[:, b, 0:n]).then_inc(S.chain_r, 1)
                dve.wait_ge(S.chain_r, r + 1)
                dve.tensor_scalar(rank_i[:, 1, 0:n], rank_i[:, 0, 0:n], P - 1, None, ALU.bitwise_and).then_inc(S.chain_r, 1)
                dve.tensor_scalar(rank_i[:, 2, 0:n], rank_i[:, 0, 0:n], 7, None, ALU.arith_shift_right).then_inc(S.chain_r, 1)
                dve.wait_ge(S.chain_r, r + 3)
                dve.scalar_tensor_tensor(out=slot_all[:, ds(k0, n)], in0=rank_i[:, 1, 0:n], scalar=float(ET),
                                         in1=rank_i[:, 2, 0:n], op0=ALU.mult, op1=ALU.add).then_inc(S.slot_ready, 1)

            with nc.vector.Fori(0, NCH // 2) as i:
                for b in range(2):
                    slots(2 * i + b, b, (2 * i + b) * CH, CH)
            slots(NCH, 0, EF, 1)
            dve.wait_ge(S.ranks_all, 1)

            def normalise(src, landed, chain, m, std_ready, dst, done):
                for j in range(G):
                    landed(j)
                    dve.bn_stats(st[:, j, :], src[:, j, :]).then_inc(chain, 1)
                for j in range(G):
                    hold(dve, chain, m * KN + j + 1)
                    dve.bn_aggr(mv[:, j, :], st[:, j, :]).then_inc(chain, 1)
                hold(dve, std_ready, m + 1)
                dve.reciprocal(rs[:, :], sd[:, :]).then_inc(chain, 1)
                hold(dve, chain, m * KN + KN)
                for j in range(G):
                    dve.tensor_scalar(dst[:, j, :], src[:, j, :], mv[:, j, 0:1], rs[:, j:j + 1],
                                      ALU.subtract, ALU.mult).then_inc(done, 1)

            with nc.vector.Fori(0, NG) as i:
                normalise(xin, lambda j: hold(dve, rows_landed[j], (i + 1) * 16), S.chain_in, i, S.std_ready, x0, S.x0_ready)
                for j in range(G):
                    n = i * G + j
                    hold(dve, S.proj_done, n + 1)
                    hold(dve, h_stored[j], (i + 1) * 16)
                    dve.tensor_tensor(hout[:, j, :], bank[j][:, 0:D], b_in[:, :], ALU.add).then_inc(S.hout_ready, 1)

            def q_phase(l):
                hold(dve, S.wl_landed, (l + 1) * 16 * NWL)
                dve.tensor_scalar(bq8[:, :], bq[:, :], 1.0 / 8.0, None, ALU.mult).then_inc(S.bias_ready, 1)
                with nc.vector.Fori(0, NG) as i:
                    for j in range(G):
                        n = l * NT + i * G + j
                        hold(dve, S.kvp_done, n + 1)
                        hold(dve, kvo_stored[j], (l * NG + i + 1) * 16)
                        dve.tensor_tensor(kvout[:, j, :], bank[5 + j % 3][:, :], bkv[:, :], ALU.add).then_inc(S.kvp_ready, 1)

            KE = 4

            def softmax(l, i, b, first):
                n = l * NB + i * TURN + b
                p, q = b % 2, (b % 2) * 2
                c = n * KE
                dve.wait_ge(S.score_done, n + 1)
                for h2 in range(2):
                    dve.tensor_reduce(
                        sc[:, p, 2 * h2:2 * h2 + 2], bank[q + h2][:, :].rearrange("p (t g s h) -> p t h g s", t=2, g=H, s=W),
                        AX.X, ALU.max).then_inc(S.score_read, 1)
                dve.wait_ge(S.score_read, 2 * n + 6)
                dve.tensor_reduce(mx[:, p], sc[:, p], AX.X, ALU.max).then_inc(S.chain_e, 1)
                dve.wait_ge(S.chain_e, c + 1)
                dve.tensor_tensor(sx[:, p], sc[:, p], mx[:, p].unsqueeze(3).to_broadcast([P, UB, H, H]),
                                  ALU.subtract).then_inc(S.exp_in, 1)
                if not first:
                    sums(l, i * TURN + b - 2, p)
                dve.wait_ge(S.exp_out, n + 1)
                dve.reduce_sum(sm[:, p], ex[:, p], AX.X).then_inc(S.chain_e, 1)
                dve.wait_ge(S.chain_e, c + 2)
                dve.reciprocal(rc[:, p], sm[:, p]).then_inc(S.chain_e, 1)
                dve.wait_ge(S.chain_e, c + 3)
                dve.tensor_tensor(at[:, p], ex[:, p], rc[:, p].unsqueeze(3).to_broadcast([P, UB, H, H]),
                                  ALU.mult).then_inc(S.chain_e, 1)
                dve.wait_ge(S.chain_e, c + 4)
                dve.tensor_tensor(
                    att[:, p].rearrange("p t s h g -> p t s (h g)"),
                    at[:, p].rearrange("p t h g -> p t (h g)").unsqueeze(2).to_broadcast([P, UB, W, H * H]),
                    onehot[:, ds((i * TURN + b) * UB, UB), :].unsqueeze(3).to_broadcast([P, UB, W, H * H]),
                    ALU.mult).then_inc(S.att_ready, 1)

            def sums(l, m, p):
                n = l * NB + m
                dve.load(wreg, wid[0:1, ds(m * UB, UB)])
                dve.wait_ge(S.agg_done, n + 1 + TURN)
                for u in range(UB):
                    w = dve.snap(wreg[u])
                    a = acc[:, ds(w, 1), :].squeeze(1)
                    dve.tensor_tensor(a, bank[6 + p][0:DH, u * 64:(u + 1) * 64], a, ALU.add).then_inc(S.chain_a, 1)
                    hold(dve, S.chain_a, n * UB + u + 1)

            def e_phase(l):
                hold(dve, S.sums_zeroed, l + 1)
                for b in range(TURN):
                    softmax(l, 0, b, b < 2)
                with nc.vector.Fori(1, NTURN) as i:
                    for b in range(TURN):
                        softmax(l, i, b, False)
                sums(l, NB - 2, 0)
                sums(l, NB - 1, 1)
                dve.sem_inc(S.edges_all, 1)

            def u_phase(l):
                hold(dve, S.ee_done, l + 1)
                dve.tensor_tensor(eewo[:, :], bank[7][0:TYPES, 0:D], bo4[:, :], ALU.add).then_inc(S.ee_ready, 1)
                with nc.vector.Fori(0, NG) as i:
                    for j in range(G):
                        n = l * NT + i * G + j
                        hold(dve, rows_landed[j], (NG * (2 + 2 * l) + i + 1) * 16)
                        hold(dve, S.upd_done, n + 1 + G)
                        dve.tensor_tensor(x0[:, j, :], bank[j][:, 0:D], xin[:, j, :], ALU.add).then_inc(S.h_u, 1)
                    hold(dve, S.h_u, (l * NG + i + 1) * G + G)
                    normalise(x0, lambda j: None, S.chain_u, l * NG + i, S.std_u, x0, S.x0_u)
                    for j in range(G):
                        n = l * NT + i * G + j
                        dve.wait_ge(S.x0_u, n + 1)
                        dve.tensor_tensor(x0[:, j, :], x0[:, j, :], lng[:, :], ALU.mult).then_inc(S.mean_u, 1)
                    for j in range(G):
                        n = l * NT + i * G + j
                        dve.wait_ge(S.mean_u, n + 1)
                        dve.tensor_tensor(x0[:, j, :], x0[:, j, :], lnb[:, :], ALU.add).then_inc(S.mean_ready, 1)
                    for j in range(G):
                        n = l * NT + i * G + j
                        dve.wait_ge(S.mean_ready, n + 1)
                        hold(dve, h_stored[j], (NG + l * NG + i + 1) * 16)
                        dve.tensor_scalar(hout[:, j, :], x0[:, j, :], 0.0, None, ALU.max).then_inc(S.hout_ready, 1)

            q_phase(0)
            dve.wait_ge(S.rec_landed, 16)
            for c in range(4):
                n = ET // 4
                t = rec[:, c * n:(c + 1) * n, 1]
                dve.tensor_tensor(onehot[:, c * n:(c + 1) * n, :],
                                  iotab[:, 0:W].unsqueeze(1).to_broadcast([P, n, W]),
                                  t.unsqueeze(2).to_broadcast([P, n, W]), ALU.is_equal).then_inc(S.onehot_ready, 1)
            wreg = [dve.alloc_register(f"wv{u}") for u in range(UB)]
            dve.wait_ge(S.wid_landed, 16)
            dve.wait_ge(S.onehot_ready, 4)
            with nc.vector.Fori(0, L - 1) as l:
                e_phase(l)
                u_phase(l)
                q_phase(l + 1)
            e_phase(L - 1)
            u_phase(L - 1)

            dve.wait_ge(S.w2_landed, 16 * len(late))
            with nc.vector.Fori(0, NG) as i:
                normalise(xo, lambda j: hold(dve, rows_landed[j], ROWS_F + (i + 1) * 32), S.chain_f, 3 * i, S.f_std, x0, S.f_x0)
                hold(dve, S.f_x0, (i + 1) * G)
                dve.tensor_tensor(x0, x0, xo, ALU.add).then_inc(S.f_xs, 1)
                hold(dve, S.f_xs, i + 2)
                dve.tensor_tensor(x0, x0, bf2[:, :].unsqueeze(1).to_broadcast([P, G, D]), ALU.add).then_inc(S.chain_y, 1)
                hold(dve, S.chain_y, i + 1)
                for j in range(G):
                    hold(dve, S.f_adj_done, i * G + j + 1)
                    hold(dve, rows_stored[j], (i + 1) * 32)
                    dve.tensor_tensor(hout[:, j, :], bank[j][:, 0:D], x0[:, j, :], ALU.add).then_inc(S.f_x1, 1)
                normalise(hout, lambda j: hold(dve, S.f_x1, i * G + j + 1), S.chain_f, 3 * i + 1, S.f_std, zb, S.f_z)
                normalise(zb, lambda j: hold(dve, S.f_z, i * G + j + 1), S.chain_f, 3 * i + 2, S.f_std, xnb, S.f_xn)
                hold(dve, S.f_lg_done, i + 1)
                dve.tensor_tensor(lg[:, ds(i * G, G), :], bank[5][:, 0:G * X].rearrange("p (j e) -> p j e", e=X),
                                  brw[:, :].unsqueeze(1).to_broadcast([P, G, X]), ALU.add).then_inc(S.f_lg_ready, 1)
            dve.wait_ge(S.f_lg_ready, NG)

            cx = [0]

            def chain(ins):
                cx[0] += 1
                ins.then_inc(S.chain_x, 1)
                dve.wait_ge(S.chain_x, cx[0])

            def wide(col):
                return col.unsqueeze(2).to_broadcast([P, NT, X])

            ix = iotax[:, :].unsqueeze(1).to_broadcast([P, NT, X])
            pr, t1, m1, m2, t2 = (small(k) for k in range(5))
            top1, i1, top2, i2, tot, inv = (cols[:, k, :] for k in range(6))
            w1c, w2c = cols[:, 6, :], cols[:, 7, :]
            chain(dve.tensor_reduce(tot, lg[:, :, :], AX.X, ALU.max))
            dve.tensor_tensor(t1, lg[:, :, :], wide(tot), ALU.subtract).then_inc(S.r_exp, 1)
            dve.wait_ge(S.r_exped, 1)
            chain(dve.reduce_sum(tot, pr, AX.X))
            chain(dve.reciprocal(inv, tot))
            chain(dve.tensor_tensor(pr, pr, wide(inv), ALU.mult))

            def pick(p, top, ind, m):
                chain(dve.tensor_reduce(top, p, AX.X, ALU.max))
                chain(dve.tensor_tensor(t1, p, wide(top), ALU.is_equal))
                chain(dve.scalar_tensor_tensor(out=t1, in0=ix, scalar=-float(X), in1=t1, op0=ALU.add, op1=ALU.mult))
                chain(dve.tensor_reduce(ind, t1, AX.X, ALU.min))
                chain(dve.tensor_scalar(ind, ind, float(X), None, ALU.add))
                chain(dve.tensor_tensor(m, ix, wide(ind), ALU.is_equal))

            pick(pr, top1, i1, m1)
            chain(dve.scalar_tensor_tensor(out=t2, in0=m1, scalar=-2.0, in1=pr, op0=ALU.mult, op1=ALU.add))
            pick(t2, top2, i2, m2)
            chain(dve.tensor_tensor(tot, top1, top2, ALU.add))
            chain(dve.reciprocal(inv, tot))
            chain(dve.tensor_tensor(w1c, top1, inv, ALU.mult))
            chain(dve.tensor_tensor(w2c, top2, inv, ALU.mult))
            va = wide(valid[:, :])
            chain(dve.tensor_tensor(m1, m1, va, ALU.mult))
            chain(dve.tensor_tensor(m2, m2, va, ALU.mult))
            chain(dve.tensor_tensor(t1, m1, m2, ALU.add))
            occ = small(5).rearrange("p t e -> p (t e)")
            inc = small(6).rearrange("p t e -> p (t e)")
            chain(dve.tensor_copy(occ.rearrange("p (e t) -> p e t", e=X), t1.rearrange("p t e -> p e t")))
            chain(dve.tensor_tensor_scan(inc, scan0[:, :], occ, 0.0, ALU.mult, ALU.add))
            chain(dve.tensor_copy(oex[:, 0], occ.rearrange("p (e t) -> p e t", e=X)))
            chain(dve.tensor_tensor(oex[:, 1].rearrange("p e t -> p (e t)"), inc, occ, ALU.subtract))
            dve.sem_inc(S.r_occ, 1)
            dve.wait_ge(S.r_rank, 1)
            cnt = bank[6][:, 256:256 + X]
            chain(dve.tensor_scalar(et_i[:, 0, :], cnt, float(P - 1), None, ALU.add))
            chain(dve.tensor_scalar(et_i[:, 1, :], et_i[:, 0, :], 7, None, ALU.arith_shift_right))
            chain(dve.tensor_copy(et[:, 0, :], et_i[:, 1, :]))
            chain(dve.tensor_tensor_scan(et[:, 1, :], wt_one[:, 0:X], et[:, 0, :], 0.0, ALU.mult, ALU.add))
            chain(dve.tensor_tensor(et[:, 2, :], et[:, 1, :], et[:, 0, :], ALU.subtract))
            chain(dve.tensor_scalar(et[:, 3, :], et[:, 2, :], float(P), None, ALU.mult))
            chain(dve.tensor_scalar(et[:, 4, :], et[:, 2, :], tileid0[:, :], None, ALU.is_le, ALU.add, accum_out=eid_f[:, :]))
            chain(dve.tensor_scalar(eid_i[:, :], eid_f[:, :], -1.0, None, ALU.add))
            pos = small(7)
            chain(dve.tensor_tensor(pos, bank[6][:, 0:NT * X].rearrange("p (e t) -> p t e", e=X),
                                    et[:, 3, :].unsqueeze(1).to_broadcast([P, NT, X]), ALU.add))
            for k, m in enumerate((m1, m2)):
                chain(dve.tensor_tensor(t1, m, pos, ALU.mult))
                chain(dve.reduce_sum(slot_f[:, k, :], t1, AX.X))
            chain(dve.tensor_copy(slot2[:, :, :], slot_f[:, :, :]))
            chain(dve.tensor_scalar(tok_at[:, 0], slot2[:, :, :], P - 1, None, ALU.bitwise_and))
            chain(dve.tensor_scalar(tok_at[:, 1], slot2[:, :, :], 7, None, ALU.arith_shift_right))
            dve.scalar_tensor_tensor(out=tok_at[:, 2], in0=tok_at[:, 0], scalar=float(MT), in1=tok_at[:, 1],
                                     op0=ALU.mult, op1=ALU.add).then_inc(S.r_slots, 1)

            with nc.vector.Fori(0, MT // 2) as i:
                for p in range(2):
                    m = 2 * i + p
                    hold(dve, S.m_y_done, m + 3)
                    hold(dve, y_stored[p], (i + 1) * 16)
                    dve.tensor_tensor(hout[:, p, :], bank[5 + p][:, 0:D], w1s[:, p, PACK - D:PACK], ALU.add).then_inc(S.m_y_ready, 1)

            dve.sem_inc(S.c_out, G)
            with nc.vector.Fori(0, NG) as i:
                for j in range(G):
                    n = i * G + j
                    hold(dve, rows_landed[j], ROWS_C + (i + 1) * 16)
                    hold(dve, gathered[j], L * NTURN * 16 + (i + 1) * 32)
                    dve.scalar_tensor_tensor(out=x0[:, j, :], in0=zb[:, j, :], scalar=wcol[:, j, 0:1], in1=xo[:, j, :],
                                             op0=ALU.mult, op1=ALU.add).then_inc(S.c_part, 1)
                for j in range(G):
                    n = i * G + j
                    hold(dve, S.c_part, n + 1 + G)
                    hold(dve, rows_stored[j], NG * 32 + 32 + i * 16)
                    dve.scalar_tensor_tensor(out=xin[:, j, :], in0=xnb[:, j, :], scalar=wcol[:, j, 1:2], in1=x0[:, j, :],
                                             op0=ALU.mult, op1=ALU.add).then_inc(S.c_out, 1)

        @block.scalar
        def _(act):
            for c in range(7):
                n = min(4, NT - 4 * c)
                act.wait_ge(S.cnt_done, c + 1)
                act.activation(cntT[:, 4 * c:4 * c + n, :], bank[6 + c % 2][0:TYPES, 0:n * P].rearrange("p (t n) -> p t n", n=P),
                               ACT.Copy).then_inc(S.cnt_copied, 1)

            with nc.scalar.Fori(0, NG) as i:
                hold(act, S.chain_in, i * KN + 2 * G)
                act.activation(sd[:, :], mv[:, :, 1], ACT.Sqrt, bias=epsc[:, :]).then_inc(S.std_ready, 1)
                for j in range(G):
                    n = i * G + j
                    hold(act, S.xT_done, n + 1)
                    act.activation(xT[:, j, :, :], bank[j][:, D:2 * D].rearrange("p (c n) -> p c n", n=P),
                                   ACT.Copy).then_inc(S.xT_ready, 1)

            def q_phase(l):
                hold(act, S.bias_ready, l + 1)
                with nc.scalar.Fori(0, NG) as i:
                    for j in range(G):
                        n = l * NT + i * G + j
                        hold(act, S.hT_done, n + 1 + G)
                        act.activation(xT[:, j, :, :], bank[j][:, 0:D].rearrange("p (c n) -> p c n", n=P),
                                       ACT.Copy).then_inc(S.hT_ready, 1)
                    for j in range(G):
                        n = l * NT + i * G + j
                        hold(act, S.q_done, n + 1)
                        for h in range(H):
                            r = (h % 2) * DH
                            ins = act.activation(
                                qt[:, ds((i * G + j) * (P // W), P // W), :].rearrange("p w (s h) -> p w s h", h=H)[:, :, :, h],
                                bank[j][r:r + DH, D + (h // 2) * P:D + (h // 2 + 1) * P].rearrange("p (w s) -> p w s", s=W),
                                ACT.Identity, bias=bq8[r:r + DH, h // 2:h // 2 + 1], scale=0.125)
                        ins.then_inc(S.q_ready, 1)

            def e_phase(l):
                def tiles(i, b, us):
                    for u in us:
                        t = l * ET + (i * TURN + b) * UB + u
                        hold(act, S.kT_done, t + 1)
                        act.activation(kt_s[:, u % 2, :, :], bank[4 + u % 2][:, 0:D].rearrange("p (c n) -> p c n", n=P), ACT.Copy)
                        w = act.snap(areg[u])
                        q = qt[:, ds(w, 1), :].squeeze(1)
                        act.activation(qbd[0:DH, u % 2, 0:64], q, ACT.Copy)
                        act.activation(qbd[DH:P, u % 2, 64:128], q, ACT.Copy).then_inc(S.kT_ready, 1)

                def exps(n, p):
                    hold(act, S.exp_in, n + 1)
                    act.activation(ex[:, p], sx[:, p], ACT.Exp).then_inc(S.exp_out, 1)

                def batch(i, b, first):
                    act.load(areg, wid[0:1, ds((i * TURN + b) * UB, UB)])
                    tiles(i, b, (0, 1))
                    if not first:
                        exps(l * NB + i * TURN + b - 1, (b + 1) % 2)
                    tiles(i, b, (2, 3))

                for b in range(TURN):
                    batch(0, b, b == 0)
                with nc.scalar.Fori(1, NTURN) as i:
                    for b in range(TURN):
                        batch(i, b, False)
                exps(l * NB + NB - 1, 1)

            def u_phase(l):
                hold(act, S.edges_all, l + 1)
                with nc.scalar.Fori(0, NG) as i:
                    for j in range(G):
                        for r in range(2):
                            ins = act.activation(
                                aggT[r * DH:(r + 1) * DH, j, :, :].rearrange("p c (w s) -> p c w s", s=W),
                                acc[:, ds((i * G + j) * (P // W), P // W), :].rearrange("p w (s c r) -> p c w s r", c=KC, r=2)[:, :, :, :, r],
                                ACT.Copy)
                        ins.then_inc(S.sums_copied, 1)
                    hold(act, S.chain_u, (l * NG + i) * KN + 2 * G)
                    act.activation(sd[:, :], mv[:, :, 1], ACT.Sqrt, bias=epsc[:, :]).then_inc(S.std_u, 1)

            q_phase(0)
            for c in range(NOB):
                act.wait_ge(S.oht_done, c + 1)
                n = min(8, ET // TG - 8 * c)
                act.activation(ohT[:, 8 * c:8 * c + n, :], bank_b[c % 2][:, 0:n * P].rearrange("p (t n) -> p t n", n=P),
                               ACT.Copy).then_inc(S.oht_copied, 1)
            areg = [act.alloc_register(f"wa{u}") for u in range(UB)]
            act.wait_ge(S.wid_landed, 16)
            act.wait_ge(S.chain_s, 3)
            with nc.scalar.Fori(0, L - 1) as l:
                e_phase(l)
                u_phase(l)
                q_phase(l + 1)
            e_phase(L - 1)
            u_phase(L - 1)

            with nc.scalar.Fori(0, NG) as i:
                def turned(done, off, to, ready):
                    for j in range(G):
                        hold(act, done, i * G + j + 1 + off)
                        act.activation(to[:, j, :, :], bank[j][:, 0:D].rearrange("p (c n) -> p c n", n=P), ACT.Copy).then_inc(ready, 1)

                def std(k):
                    hold(act, S.chain_f, (3 * i + k) * KN + 2 * G)
                    act.activation(sd[:, :], mv[:, :, 1], ACT.Sqrt, bias=epsc[:, :]).then_inc(S.f_std, 1)

                turned(S.f_hT_done, G, xT, S.f_xT_ready)
                std(0)
                for j in range(G):
                    hold(act, S.f_u_done, i * G + j + 1)
                    for c in range(KC):
                        ins = act.activation(rT[:, j, c, :], bank[j][:, D + c * P:D + (c + 1) * P], ACT.Relu, bias=bf1[:, c:c + 1])
                    ins.then_inc(S.f_r_ready, 1)
                std(1)
                for j in range(G):
                    hold(act, S.f_zT_done, i * G + j + 1)
                    act.activation(xT[:, j, :, :], bank[j][:, D:2 * D].rearrange("p (c n) -> p c n", n=P), ACT.Copy).then_inc(S.f_zT_ready, 1)
                std(2)
            act.wait_ge(S.r_exp, 1)
            act.activation(small(0), small(1), ACT.Exp).then_inc(S.r_exped, 1)

            o_g = KC * HID

            def gelu(i, p):
                m = 2 * i + p
                hold(act, S.m_h_done, m + 1)
                for c in range(HC):
                    ins = act.activation(hs[:, p, c, :], bank[1 + 2 * p + c // 4][:, (c % 4) * P:(c % 4 + 1) * P], ACT.Gelu,
                                         bias=w1s[:, p, o_g + 2 * KC + c:o_g + 2 * KC + c + 1])
                ins.then_inc(S.m_h_ready, 1)

            def affine(i, p):
                m = 2 * i + p
                hold(act, S.m_xT_done, m + 1)
                hold(act, m_w1_landed[p], (i + 1) * 16)
                for c in range(KC):
                    ins = act.activation(xT[:, p, c, :], bank[0][:, p * D + c * P:p * D + (c + 1) * P], ACT.Identity,
                                         scale=w1s[:, p, o_g + c:o_g + c + 1], bias=w1s[:, p, o_g + KC + c:o_g + KC + c + 1])
                ins.then_inc(S.m_xe_ready, 1)

            affine(0, 0)
            with nc.scalar.Fori(0, MT // 2 - 1) as i:
                affine(i, 1)
                gelu(i, 0)
                affine(i + 1, 0)
                gelu(i, 1)
            affine(MT // 2 - 1, 1)
            gelu(MT // 2 - 1, 0)
            gelu(MT // 2 - 1, 1)

        @block.tensor
        def _(pe):
            pe.wait_ge(S.const_landed, 16 * nconst)
            pe.wait_ge(S.start_ready, 1)
            mm = pe.matmul
            for b in range(2):
                mm(bank[b][:, 0:NT * TYPES], zerob[:, :], iotab[:, 0:NT * TYPES], start=True, stop=False, skip_group_check=True)

            def hist(c, b, n):
                pe.wait_ge(S.ohlo_ready, c + 1)
                pe.wait_ge(S.ohcode_ready, c + 1)
                for k in range(n):
                    ins = mm(bank[k % 2][:, 0:NT * TYPES], oh_lo[:, b, k, :], oh_code[:, b, k, :],
                             start=False, stop=False, skip_group_check=True)
                ins.then_inc(S.hist_used, 1)

            with nc.tensor.Fori(0, NCH // 2) as i:
                for b in range(2):
                    hist(2 * i + b, b, CH)
            hist(NCH, 0, 1)
            for b in range(2):
                ins = mm(bank[b][:, 0:NT * TYPES], zerob[:, :], iotab[:, 0:NT * TYPES], start=False, stop=True, skip_group_check=True)
            ins.then_inc(S.hist_done, 1)
            pe.wait_ge(S.hist_copied, 1)
            for a in range(2):
                for q in range(P // W):
                    ins = mm(bank[2 + a][:, q:NW:P // W], selq[:, q, :], cnt_hi[:, a, :], start=True, stop=True, skip_group_check=True)
            ins.then_inc(S.wincnt_done, 1)
            for c in range(7):
                n = min(4, NT - 4 * c)
                if c >= 2:
                    pe.wait_ge(S.cnt_copied, c - 1)
                for k in range(n):
                    ins = pe.transpose(bank[6 + c % 2][0:TYPES, k * P:(k + 1) * P], cnt4[:, 4 * c + k, :], ident[:, :])
                ins.then_inc(S.cnt_done, 1)
            pe.wait_ge(S.base_ready, 1)
            for a in range(2):
                mm(bank[4 + a][:, 0:NW], onesrow[:, :], wt_base[0:1, a, :], start=True, stop=False, skip_group_check=True)

            def ranks(c, b, n):
                pe.wait_ge(S.ohwin_ready, c + 1)

                def after(k):
                    pe.wait_ge(S.rank_read, c * CH + k + 1)
                    return mm(bank[4 + k % 2][:, 0:NW], notbelow[:, :], oh_win[:, b, k, :],
                              start=False, stop=False, skip_group_check=True)

                for k in range(n):
                    mm(bank[4 + k % 2][:, 0:NW], below[:, :], oh_win[:, b, k, :],
                       start=False, stop=False, skip_group_check=True).then_inc(S.rank_ready, 1)
                    if k:
                        after(k - 1)
                return after(n - 1)

            with nc.tensor.Fori(0, NCH // 2) as i:
                for b in range(2):
                    ranks(2 * i + b, b, CH)
            ranks(NCH, 0, 1).then_inc(S.ranks_all, 1)

            with nc.tensor.Fori(0, NG) as i:
                for j in range(G):
                    n = i * G + j
                    pe.wait_ge(S.x0_ready, n + 1 + G)
                    for c in range(KC):
                        ins = pe.transpose(bank[j][:, D + c * P:D + (c + 1) * P], x0[:, j, c * P:(c + 1) * P], ident[:, :])
                    ins.then_inc(S.xT_done, 1)
                for j in range(G):
                    n = i * G + j
                    pe.wait_ge(S.xT_ready, n + 1)
                    for c in range(KC):
                        ins = mm(bank[j][:, 0:D], xT[:, j, c, :], w_in[:, c, :], start=(c == 0), stop=(c == KC - 1))
                    ins.then_inc(S.proj_done, 1)

            def q_phase(l):
                hold(pe, S.wl_landed, (l + 1) * 16 * NWL)
                with nc.tensor.Fori(0, NG) as i:
                    for j in range(G):
                        n = l * NT + i * G + j
                        pe.wait_ge(rows_landed[j], (NG * (1 + 2 * l) + i + 1) * 16)
                        pe.wait_ge(S.q_ready, n + 1)
                        for c in range(KC):
                            ins = pe.transpose(bank[j][:, c * P:(c + 1) * P], xin[:, j, c * P:(c + 1) * P], ident[:, :])
                        ins.then_inc(S.hT_done, 1)
                    for j in range(G):
                        n = l * NT + i * G + j
                        pe.wait_ge(S.hT_ready, n + 1)
                        for a in range(KC):
                            for c in range(KC):
                                ins = mm(bank[j][:, D + a * P:D + (a + 1) * P], wq[:, c, a * P:(a + 1) * P], xT[:, j, c, :],
                                         start=(c == 0), stop=(c == KC - 1), skip_group_check=True)
                        ins.then_inc(S.q_done, 1)
                        pe.wait_ge(S.kvp_ready, n + 1)
                        for c in range(KC):
                            ins = mm(bank[5 + j % 3][:, :], xT[:, j, c, :], wkv[:, c, :], start=(c == 0), stop=(c == KC - 1))
                        ins.then_inc(S.kvp_done, 1)
                hold(pe, S.q_ready, (l + 1) * NT + G)

            def e_phase(l):
                def scores(i, b):
                    n = l * NB + i * TURN + b

                    def turn_keys(u):
                        t = n * UB + u
                        pe.wait_ge(gathered[b * UB + u], (l * NTURN + i + 1) * 16)
                        for c in range(KC):
                            ins = pe.transpose(bank[4 + u % 2][:, c * P:(c + 1) * P], kv[:, b, u, c * P:(c + 1) * P], ident[:, :])
                        ins.then_inc(S.kT_done, 1)

                    turn_keys(0)
                    for u in range(UB):
                        if u + 1 < UB:
                            turn_keys(u + 1)
                        bk = bank[2 * (b % 2) + u // 2][:, (u % 2) * D:(u % 2 + 1) * D]
                        pe.wait_ge(S.score_read, 2 * n + 1 + u // 2)
                        mm(bk, ohT[:, ds(i * 2 + b // 2, 1), :].squeeze(1), maskc[:, (b % 2) * UB + u, :],
                           start=True, stop=False, skip_group_check=True)
                        pe.wait_ge(S.kT_ready, n * UB + u + 1)
                        for c in range(KC):
                            ins = mm(bk[:, c * P:(c + 1) * P], kt_s[:, u % 2, c, :], qbd[:, u % 2, :],
                                     start=False, stop=(c == KC - 1), skip_group_check=True)
                    ins.then_inc(S.score_done, 1)

                def aggregate(n, b):
                    pe.wait_ge(S.att_ready, n + 1)
                    for u in range(UB):
                        for g in range(H):
                            ins = mm(bank[6 + b % 2][0:DH, u * 64:(u + 1) * 64], kv[:, b, u, D + g * DH:D + (g + 1) * DH],
                                     att[:, b % 2, u, :, :, g].rearrange("p s h -> p (s h)"),
                                     start=(g == 0), stop=(g == H - 1), skip_group_check=True)
                    ins.then_inc(S.agg_done, 1)

                for b in range(TURN):
                    scores(0, b)
                    if b:
                        aggregate(l * NB + b - 1, b - 1)
                with nc.tensor.Fori(1, NTURN) as i:
                    for b in range(TURN):
                        scores(i, b)
                        aggregate(l * NB + i * TURN + b - 1, (b - 1) % TURN)
                aggregate(l * NB + NB - 1, TURN - 1)

            def u_phase(l):
                hold(pe, S.edges_all, l + 1)
                for c in range(KC):
                    ins = mm(bank[7][0:TYPES, 0:D], eeT[:, c, :], wo[:, c, :], start=(c == 0), stop=(c == KC - 1))
                ins.then_inc(S.ee_done, 1)
                hold(pe, S.ee_ready, l + 1)
                with nc.tensor.Fori(0, NG) as i:
                    for j in range(G):
                        n = l * NT + i * G + j
                        pe.wait_ge(S.sums_copied, n + 1 + NT)
                        pe.wait_ge(S.cnts_ready, n + 1)
                        pe.wait_ge(S.h_u, n + 1)
                        for c in range(KC):
                            mm(bank[j][:, 0:D], aggT[:, j, c, :], wo[:, c, :], start=(c == 0), stop=False)
                        mm(bank[j][:, 0:D], cnt_s[:, j, :], eewo[:, :], start=False, stop=True).then_inc(S.upd_done, 1)

            q_phase(0)
            pe.wait_ge(S.onehot_ready, 4)
            for c in range(NOB):
                if c >= 2:
                    pe.wait_ge(S.oht_copied, c - 1)
                for k in range(min(8, ET // TG - 8 * c)):
                    t = (8 * c + k) * TG
                    ins = pe.transpose(bank_b[c % 2][:, k * P:(k + 1) * P],
                                       onehot[:, t:t + TG, :].rearrange("p t s -> p (t s)"), identb[:, :])
                ins.then_inc(S.oht_done, 1)
            pe.wait_ge(S.oht_copied, NOB)
            with nc.tensor.Fori(0, L - 1) as l:
                e_phase(l)
                u_phase(l)
                q_phase(l + 1)
            e_phase(L - 1)
            u_phase(L - 1)

            pe.wait_ge(S.w2_landed, 16 * len(late))
            with nc.tensor.Fori(0, NG) as i:
                for j in range(G):
                    pe.wait_ge(rows_landed[j], ROWS_F + (i + 1) * 32)
                    for c in range(KC):
                        ins = pe.transpose(bank[j][:, c * P:(c + 1) * P], xin[:, j, c * P:(c + 1) * P], ident[:, :])
                    ins.then_inc(S.f_hT_done, 1)
                for j in range(G):
                    pe.wait_ge(S.f_xT_ready, i * G + j + 1)
                    for a in range(KC):
                        for c in range(KC):
                            ins = mm(bank[j][:, D + a * P:D + (a + 1) * P], wf1[:, c, a * P:(a + 1) * P], xT[:, j, c, :],
                                     start=(c == 0), stop=(c == KC - 1), skip_group_check=True)
                    ins.then_inc(S.f_u_done, 1)
                for j in range(G):
                    pe.wait_ge(S.f_r_ready, i * G + j + 1)
                    for c in range(KC):
                        ins = mm(bank[j][:, 0:D], rT[:, j, c, :], wf2[:, c, :], start=(c == 0), stop=(c == KC - 1), skip_group_check=True)
                    ins.then_inc(S.f_adj_done, 1)
                for j in range(G):
                    pe.wait_ge(S.f_z, i * G + j + 1)
                    for c in range(KC):
                        ins = pe.transpose(bank[j][:, D + c * P:D + (c + 1) * P], zb[:, j, c * P:(c + 1) * P], ident[:, :])
                    ins.then_inc(S.f_zT_done, 1)
                for j in range(G):
                    pe.wait_ge(S.f_zT_ready, i * G + j + 1)
                    for c in range(KC):
                        ins = mm(bank[5][:, j * X:(j + 1) * X], xT[:, j, c, :], wr[:, c, :], start=(c == 0), stop=(c == KC - 1),
                                 skip_group_check=True)
                ins.then_inc(S.f_lg_done, 1)
            pe.wait_ge(S.r_occ, 1)
            o0, o1 = (oex[:, k].rearrange("p e t -> p (e t)") for k in range(2))
            mm(bank[6][:, 0:NT * X], below[:, :], o0, start=True, stop=False, skip_group_check=True)
            mm(bank[6][:, 0:NT * X], onesb[:, :], o1, start=False, stop=True, skip_group_check=True)
            mm(bank[6][:, 256:256 + X], onesb[:, :], oex[:, 0, :, NT - 1], start=True, stop=False, skip_group_check=True)
            mm(bank[6][:, 256:256 + X], onesb[:, :], oex[:, 1, :, NT - 1], start=False, stop=True,
               skip_group_check=True).then_inc(S.r_rank, 1)

            def hidden(i, p):
                m = 2 * i + p
                pe.wait_ge(gathered[G + p], (L * NTURN + i + 1) * 16)
                for c in range(KC):
                    ins = pe.transpose(bank[0][:, p * D + c * P:p * D + (c + 1) * P], xin[:, p, c * P:(c + 1) * P], ident[:, :])
                ins.then_inc(S.m_xT_done, 1)
                pe.wait_ge(S.m_xe_ready, m + 1)
                for h in range(HC):
                    for c in range(KC):
                        ins = mm(bank[1 + 2 * p + h // 4][:, (h % 4) * P:(h % 4 + 1) * P], w1s[:, p, c * HID + h * P:c * HID + (h + 1) * P],
                                 xT[:, p, c, :], start=(c == 0), stop=(c == KC - 1), skip_group_check=True)
                ins.then_inc(S.m_h_done, 1)

            preg = [pe.alloc_register(f"wp{p}") for p in range(2)]

            def outputs(i, p):
                m = 2 * i + p
                e = pe.snap(preg[p])
                pe.wait_ge(S.m_h_ready, m + 1)
                for h in range(HC):
                    ins = mm(bank[5 + p][:, 0:D], hs[:, p, h, :], w2r[:, ds(e, 1), h, :].squeeze(1), start=(h == 0), stop=(h == HC - 1))
                ins.then_inc(S.m_y_done, 1)

            pe.wait_ge(S.eid_landed, 16)
            hidden(0, 0)
            with nc.tensor.Fori(0, MT // 2 - 1) as i:
                pe.load(preg, eid[0:1, ds(2 * i, 2)])
                hidden(i, 1)
                outputs(i, 0)
                hidden(i + 1, 0)
                outputs(i, 1)
            pe.load(preg, eid[0:1, MT - 2:MT])
            hidden(MT // 2 - 1, 1)
            outputs(MT // 2 - 1, 0)
            outputs(MT // 2 - 1, 1)


def constants():
    bf = mybir.dt.np(BF16)
    r = np.arange(P)
    before = (r[:, None] < r[None, :])
    selq = np.zeros((P, P // W, P), np.float32)
    selq[r, r // W, :] = 1
    mask = np.zeros((TG, W, TG, H, W, H), np.float32)
    for t in range(TG):
        for s in range(W):
            mask[t, s, t] = -BIG
            mask[t, s, t, :, s, :] = 0
    return {
        "c_ident": np.eye(P, dtype=np.float32), "c_identb": np.eye(P, dtype=bf),
        "c_below": before.astype(bf), "c_notbelow": (~before).astype(bf), "c_selq": selq,
        "c_iota": np.broadcast_to(np.arange(NW), (P, NW)).astype(bf),
        "c_tileid": np.arange(P * 5, dtype=np.float32).reshape(P, 5),
        "c_mask": mask.reshape(P, TG, D).astype(bf), "c_ones": np.ones((1, P), np.float32),
        "c_zero": np.zeros((P, P), bf), "c_onesb": np.ones((P, P), bf),
        "c_valid": (r[:, None] + P * np.arange(NT) < N).astype(np.float32),
        "c_tokid": (r[:, None] + P * np.arange(NT)).astype(np.int32),
        "c_tile0": r.astype(np.float32)[:, None],
        "c_iotax": np.broadcast_to(np.arange(X, dtype=np.float32), (P, X)),
        "c_scan0": np.broadcast_to(np.tile(np.arange(NT) > 0, X).astype(np.float32), (P, X * NT)),
    }


def layout(v):
    def kt(w):
        w = np.swapaxes(w, -1, -2)
        w = w.reshape(*w.shape[:-2], KC, P, w.shape[-1])
        return np.swapaxes(w, -2, -3)

    def wide(b):
        return np.broadcast_to(b[..., None, :], (*b.shape[:-1], P, b.shape[-1]))

    x = np.zeros((NP, D), np.float32)
    x[:N] = v["x"]
    edges = np.zeros((P, 3, EC), np.int32)
    edges[:, 0, EF] = 4095
    for k, name in enumerate(("src", "dst", "edge_type_3")):
        edges[:, k, :EF] = v[name][:EF * P].reshape(P, EF)
        edges[:ER, k, EF] = v[name][EF * P:]
    g = {k[7:]: np.asarray(a) for k, a in v.items() if k.startswith("L0_gnn_")}
    bo4 = np.zeros((L, TYPES, D), np.float32)
    bo4[:, TYPES - 1] = g["bo"]
    ee = np.zeros((L, TYPES, D), np.float32)
    ee[:, :3] = g["Eemb"]
    f = {k[7:]: np.asarray(a) for k, a in v.items() if k.startswith("L0_ffn_")}
    pack = np.concatenate([
        f["W1"].reshape(X, KC, P, HID).transpose(0, 2, 1, 3).reshape(X, P, KC * HID),
        f["ln_g"].reshape(X, KC, P).transpose(0, 2, 1), f["ln_b"].reshape(X, KC, P).transpose(0, 2, 1),
        f["b1"].reshape(X, HC, P).transpose(0, 2, 1), wide(f["b2"])], -1)
    return {
        "wf1": kt(g["W1"]), "wf2": kt(g["W2"]), "bf1": g["b1"].reshape(KC, P).T, "bf2": wide(g["b2"]),
        "wr": f["Wr"].reshape(KC, P, X).transpose(1, 0, 2), "br": wide(f["br"]), "pack": pack,
        "w2": f["W2"].reshape(X, HC, P, D).transpose(2, 0, 1, 3),
        "x": x, "edges": edges, "win": kt(g["Win"]), "b_in": wide(g["b_in"]),
        "wq": kt(g["Wq"]), "bq": np.swapaxes(g["bq"].reshape(L, KC, P), 1, 2),
        "wkv": np.concatenate([kt(g["Wk"]), kt(g["Wv"])], -1), "bkv": wide(np.concatenate([g["bk"], g["bv"]], -1)),
        "wo": kt(g["Wo"]), "eeT": kt(ee), "bo4": bo4, "lng": wide(g["ln_g"]), "lnb": wide(g["ln_b"]),
    }


def kernel(**inputs):
    import concourse.bacc as _bacc
    from concourse.bass_utils import run_bass_kernel_spmd as _run

    v = {k: np.asarray(a) for k, a in inputs.items()}
    nc = _bacc.Bacc("TRN2", target_bir_lowering=False, num_devices=1)
    arrays, aps = {}, {}
    for name, a in {**layout(v), **constants()}.items():
        arrays["in_" + name] = np.ascontiguousarray(a)
        aps[name] = nc.dram_tensor("in_" + name, a.shape, mybir.dt.from_np(a.dtype), kind="ExternalInput").ap()
    out = nc.dram_tensor("out", (NP, D), F32, kind="ExternalOutput").ap()
    build(nc, namedtuple("Inputs", aps)(**aps), out)
    r = _run(nc, [arrays], core_ids=[0])
    return r.results[0]["out"][:N]
```
